# Optimizing a Trainium2 kernel written in Bass

```python
import numpy as np
import jax
import jax.numpy as jnp

def _softmax(x, axis=-1):
    return jax.nn.softmax(x, axis=axis)
def _gelu(x):
    return jax.nn.gelu(x, approximate=True)
def _silu(x):
    return jax.nn.silu(x)
def _sigmoid(x):
    return jax.nn.sigmoid(x)
def _layernorm(x, axis=-1, eps=1e-5):
    m = jnp.mean(x, axis=axis, keepdims=True)
    v = jnp.var(x, axis=axis, keepdims=True)
    return (x - m) / jnp.sqrt(v + eps)
def _scatter_add(tgt, idx, src, axis=0):
    return tgt.at[idx].add(src)
def _segment_sum(src, seg, n):
    return jax.ops.segment_sum(src, seg, n)

kernel_name = 'mk_conv_preact_d1_conv_nchw384_f7a290'

def setup_inputs(seed: int = 0):
    np.random.seed(seed)
    _w = jnp.asarray
    def _rec_inputs():
        import jax
        import jax.numpy as jnp
        _gk = jax.random.key(seed)
        x = 7.572e-06 + 1 * jax.random.normal(jax.random.fold_in(_gk, 1), (32, 384, 28, 28), jnp.float32)
        return x
    x = _rec_inputs()
    def _L0_conv_setup():
        import jax, jax.numpy as jnp
        import numpy as np
        B, C, H, W = (32, 384, 28, 28)
        E, HID, K = (4, 384, 2)
        key = jax.random.key(seed)
        ks = jax.random.split(key, 5)
        x = jax.random.normal(ks[0], (B, C, H, W), jnp.float32)
        gate_w = jax.random.normal(ks[1], (C, E), jnp.float32) * 0.02
        gate_b = jnp.zeros((E,), jnp.float32)
        w1 = jax.random.normal(ks[2], (E, HID, C), jnp.float32) * 0.02
        b1 = jnp.zeros((E, HID), jnp.float32)
        w2 = jax.random.normal(ks[3], (E, C, HID), jnp.float32) * 0.02
        b2 = jnp.zeros((E, C), jnp.float32)
        return {'x': x, 'gate_w': gate_w, 'gate_b': gate_b, 'w1': w1, 'b1': b1, 'w2': w2, 'b2': b2}
    _L0_conv_all = _L0_conv_setup()
    _L0_conv_in = {k: v for k, v in _L0_conv_all.items() if k in ('gate_w', 'gate_b', 'w1', 'b1', 'w2', 'b2', )}
    del _L0_conv_all

    return {
        "x": x,
        "L0_conv_gate_w": _L0_conv_in["gate_w"],
        "L0_conv_gate_b": _L0_conv_in["gate_b"],
        "L0_conv_w1": _L0_conv_in["w1"],
        "L0_conv_b1": _L0_conv_in["b1"],
        "L0_conv_w2": _L0_conv_in["w2"],
        "L0_conv_b2": _L0_conv_in["b2"],
    }

def reference(x, L0_conv_gate_w, L0_conv_gate_b, L0_conv_w1, L0_conv_b1, L0_conv_w2, L0_conv_b2):
    import jax
    import jax.numpy as jnp
    def _L0_conv_ref(x, gate_w, gate_b, w1, b1, w2, b2):
        import jax, jax.numpy as jnp
        import numpy as np
        B, C, H, W = (32, 384, 28, 28)
        E, HID, K = (4, 384, 2)
        b, c, h, w = x.shape
        e = gate_b.shape[0]
        x_flat = x.transpose(0, 2, 3, 1).reshape(-1, c)
        scores = jax.nn.softmax(x_flat @ gate_w + gate_b, -1)
        top_v, top_i = jax.lax.top_k(scores, K)
        top_w = jax.nn.softmax(top_v, -1)
        wmap = top_w.T.reshape(K, b, h, w)
        present = (top_i[:, :, None] == jnp.arange(e)[None, None, :]).any(0)
        coef = jnp.einsum('ke,kbhw->ebhw', present.astype(x.dtype), wmap)
        hdn = jax.nn.relu(jnp.einsum('bchw,edc->ebdhw', x, w1) + b1[:, None, :, None, None])
        y = jnp.einsum('ebdhw,eod->ebohw', hdn, w2) + b2[:, None, :, None, None]
        out = jnp.einsum('ebohw,ebhw->bohw', y, coef)
        return out

    def _gn(v, G=32, eps=1e-5):
        B_, C_, H_, W_ = v.shape
        g = v.reshape(B_, G, C_ // G, H_, W_)
        m = jnp.mean(g, axis=(2, 3, 4), keepdims=True)
        s = jnp.var(g, axis=(2, 3, 4), keepdims=True)
        return ((g - m) / jnp.sqrt(s + eps)).reshape(v.shape)

    def _ln_c(v, eps=1e-6):
        m = jnp.mean(v, axis=1, keepdims=True)
        s = jnp.var(v, axis=1, keepdims=True)
        return (v - m) / jnp.sqrt(s + eps)

    def _ln_t(v, eps=1e-5):
        m = jnp.mean(v, axis=-1, keepdims=True)
        s = jnp.var(v, axis=-1, keepdims=True)
        return (v - m) / jnp.sqrt(s + eps)

    def _to_tokens(v):
        B_, C_, H_, W_ = v.shape
        return v.reshape(B_, C_, H_ * W_).transpose(0, 2, 1)
    def _from_tokens(t, like):
        B_, C_, H_, W_ = like.shape
        return t.transpose(0, 2, 1).reshape(B_, C_, H_, W_)

    x = x + _L0_conv_ref(_gn(x), L0_conv_gate_w, L0_conv_gate_b, L0_conv_w1, L0_conv_b1, L0_conv_w2, L0_conv_b2)
    return x


_drawn_inputs = setup_inputs


def setup_inputs(seed=0):
    import zlib

    import numpy as np

    out = dict(_drawn_inputs(seed))
    spreads = {'L0_conv_gate_b': (0.0, 0.1), 'L0_conv_b1': (0.0, 0.1), 'L0_conv_b2': (0.0, 0.1)}
    factors = {}
    for name, (base, spread) in spreads.items():
        noise = np.random.default_rng([zlib.crc32(name.encode()), seed]).standard_normal(out[name].shape)
        drawn = base * np.exp(spread * noise) if base else spread * noise
        out[name] = jnp.asarray(drawn.astype(out[name].dtype))
    for name, factor in factors.items():
        out[name] = (out[name] * factor).astype(out[name].dtype)
    return out
```

```python
import concourse.bass as bass
from concourse import mybir
from contextlib import ExitStack

B, C, PIX = 32, 384, 784
E, HID = 4, 384
P = 128
NJ = C // P
NK = HID // P
HALVES = 2
T = PIX // HALVES
GROUPS_PER_32 = 8
GN_EPS = 1e-5
GP, GJ = 112, 7
ROWS = 2 + E
UNITS = HALVES * E
CHUNKS = UNITS * NK
ZB = 4
RING = 2 * NK
DVE_LINKS = 42
SCAN_LINKS = 34


def conv_moe(nc, x, gate_w, gate_b, w1, b1, w2, b2, out):
    f32, f32r, i32 = mybir.dt.float32, mybir.dt.float32r, mybir.dt.int32
    ALU, ACT, AX = mybir.AluOpType, mybir.ActivationFunctionType, mybir.AxisListType

    x_v = x.rearrange("b (p j) h w -> b p j (h w)", j=NJ)
    out_v = out.rearrange("b (p j) h w -> b p j (h w)", j=NJ)

    ctx = ExitStack()
    with ctx:
        def sb(name, shape, dt=f32):
            return ctx.enter_context(nc.sbuf_tensor(name, shape, dt))

        def pb(name, shape):
            return ctx.enter_context(nc.psum_tensor(name, shape, f32))

        def sem(name):
            return ctx.enter_context(nc.semaphore(name))

        w1_hi = sb("w1_hi", [P, E, NJ, HID], f32r)
        w1_lo = sb("w1_lo", [P, E, NJ, HID], f32r)
        w2_hi = sb("w2_hi", [P, E, NK, C], f32r)
        w2_lo = sb("w2_lo", [P, E, NK, C], f32r)
        gw_in = sb("gw_in", [P, NJ, E])
        gw = sb("gw", [P, NJ, 2, E], f32r)
        gb = sb("gb", [GP, E])
        b1_sb = sb("b1_sb", [P, E, NK])
        b2_sb = sb("b2_sb", [P, E, NJ])

        x_raw = sb("x_raw", [P, 2, NJ, PIX])
        x_hi = sb("x_hi", [P, 2, HALVES, NJ, T], f32r)
        x_lo = sb("x_lo", [P, 2, HALVES, NJ, T], f32r)
        xn = sb("xn", [P, NJ, T])
        rows = sb("rows", [P, 2, HALVES, ROWS, T])
        w1_in = rows[:, 1].rearrange("p h r t -> p (h r t)")[:, 0:E * NJ * HID]
        w2_in = rows[:, 0].rearrange("p h r t -> p (h r t)")[:, 0:E * NK * C]
        hid = sb("hid", [P, RING, T])
        h_hi = sb("h_hi", [P, RING, T], f32r)
        h_lo = sb("h_lo", [P, RING, T], f32r)

        st6 = sb("st6", [P, NJ * HALVES, 6])
        st = sb("st", [P, 2, 32])
        stT = sb("stT", [P, 2, GROUPS_PER_32, 4])
        pad = sb("pad", [1, 1])
        gsum = sb("gsum", [P, GROUPS_PER_32])
        gmean = sb("gmean", [P, GROUPS_PER_32])
        dev = sb("dev", [P, GROUPS_PER_32, 4])
        dev2 = sb("dev2", [P, GROUPS_PER_32, 4])
        gvar = sb("gvar", [P, GROUPS_PER_32])
        gvar_eps = sb("gvar_eps", [P, GROUPS_PER_32])
        minus_half = sb("minus_half", [P, GROUPS_PER_32])
        rstd = sb("rstd", [P, GROUPS_PER_32])
        back = sb("back", [P, 2, GROUPS_PER_32, 4])
        norm = sb("norm", [P, 2, 32])

        lg_rows = sb("lg_rows", [2 * E, HALVES, T])
        lg_pix = sb("lg_pix", [GP, 2 * E, GJ])
        lg = sb("lg", [GP, E, GJ])
        lg_max = sb("lg_max", [GP, GJ])
        ex = sb("ex", [GP, E, GJ])
        ssum = sb("ssum", [GP, GJ])
        score = sb("score", [GP, E, GJ])
        pair_hi = sb("pair_hi", [GP, 2, GJ])
        pair_lo = sb("pair_lo", [GP, 2, GJ])
        top1 = sb("top1", [GP, GJ])
        top2 = sb("top2", [GP, GJ])
        mid = sb("mid", [GP, 2, GJ])
        gap = sb("gap", [GP, GJ])
        zexp = sb("zexp", [GP, GJ])
        den = sb("den", [GP, GJ])
        wrow = sb("wrow", [GP, ROWS, GJ])
        wtmp = sb("wtmp", [GP, E, GJ])
        order = sb("order", [GP, E])
        pick = sb("pick", [GP, E, GJ])
        pick_max = sb("pick_max", [GP, GJ])
        onehot = sb("onehot", [GP, 2, E, GJ])
        rest = sb("rest", [GP, E, GJ])
        cnt = sb("cnt", [GP, 2 * E])
        cnt_img = sb("cnt_img", [GP, 2 * E])
        ones = sb("ones", [GP, P])
        present = sb("present", [P, 2 * E])
        fewest = sb("fewest", [P, 1])
        missing = sb("missing", [P, 1], i32)
        bias01 = sb("bias01", [P, 2, NJ])

        y_ps = pb("y_ps", [P, NJ, 512])
        z_ps = pb("z_ps", [P, ZB, 512])
        g_ps = pb("g_ps", [P, 512])

        lg_dram = nc.dram_tensor("lg_dram", (2 * E, PIX), f32).ap()
        rows_dram = nc.dram_tensor("rows_dram", (2, ROWS, PIX), f32).ap()

        small_loaded = sem("small_loaded")
        w1_loaded = [sem(f"w1_loaded{e}") for e in range(E)]
        w2_loaded = [sem(f"w2_loaded{e}") for e in range(E)]
        whi_ready = sem("whi_ready")
        wlo_ready = sem("wlo_ready")
        const_ready = sem("const_ready")
        dve_step = sem("dve_step")
        flag_ready = sem("flag_ready")
        present_ready = sem("present_ready")
        z_ready = sem("z_ready")
        relu_done = sem("relu_done")
        scaled = sem("scaled")
        hhi_ready = sem("hhi_ready")
        hlo_ready = sem("hlo_ready")
        unit_done = sem("unit_done")
        out_ready = sem("out_ready")
        stored = sem("stored")
        rows_written = sem("rows_written")
        rows_loaded = [sem("rows_loaded0"), sem("rows_loaded1")]
        gap_ready = sem("gap_ready")
        gexp_ready = sem("gexp_ready")

        class Sems:

            def __init__(self, pre):
                self.x_loaded = sem(pre + "x_loaded")
                self.var_ready = sem(pre + "var_ready")
                self.rstd_ready = sem(pre + "rstd_ready")
                self.xn_ready = sem(pre + "xn_ready")
                self.xhi_ready = sem(pre + "xhi_ready")
                self.xlo_ready = sem(pre + "xlo_ready")
                self.gate_ready = sem(pre + "gate_ready")
                self.gate_copied = sem(pre + "gate_copied")
                self.gate_written = sem(pre + "gate_written")
                self.gate_moved = sem(pre + "gate_moved")
                self.logit_ready = sem(pre + "logit_ready")
                self.exp_ready = sem(pre + "exp_ready")
                self.cnt_ready = sem(pre + "cnt_ready")
                self.cnt_summed = sem(pre + "cnt_summed")

        main = Sems("")
        scan = Sems("scan_")
        scan_step = sem("scan_step")
        scan_free = sem("scan_free")

        def half(h):
            return slice(h * T, (h + 1) * T)


        def load_x(sp, s, b, q):
            sp.dma_start(x_raw[:, q], x_v[b]).then_inc(s.x_loaded, 16)

        class Links:

            def __init__(self, eng, s, base):
                self.eng, self.s, self.base, self.n = eng, s, base, 0

            def inc(self, ins):
                self.n += 1
                ins.then_inc(self.s, 1)

            def wait(self):
                self.eng.wait_ge(self.s, self.base + self.n)

            def link(self, ins):
                self.inc(ins)
                self.wait()

        def stats_first(dve, s, n, q):
            dve.wait_ge(s.x_loaded, 16 * (n + 1))
            for i in range(3):
                nc.vector.bn_stats(st6[:, i], x_raw[:, q, i // HALVES, half(i % HALVES)])

        def stats_rest(dve, s, n, q, lk):
            for i in range(3, NJ * HALVES):
                ins = nc.vector.bn_stats(st6[:, i], x_raw[:, q, i // HALVES, half(i % HALVES)])
            lk.inc(ins)

        def group_stats(dve, s, n, lk):
            lk.wait()
            nc.vector.memset(pad[:, :], 0.0)
            lk.link(nc.vector.bn_aggr(st[:, :, 0], st6[:, :, :].rearrange("p a b -> p (a b)")))
            lk.link(nc.vector.transpose(stT[:, :, :, :].rearrange("p a g f -> p (a g f)"),
                                        st[:, :, :].rearrange("p a b -> p (a b)")))
            lk.link(nc.vector.tensor_reduce(gsum[:, :], stT[:, 0], AX.X, ALU.add))
            lk.link(nc.vector.tensor_scalar(gmean[:, :], gsum[:, :], 0.25, None, ALU.mult))
            lk.link(nc.vector.tensor_tensor(dev[:, :, :], stT[:, 0],
                                            gmean[:, :].unsqueeze(2).to_broadcast([P, GROUPS_PER_32, 4]),
                                            ALU.subtract))
            lk.link(nc.vector.tensor_tensor(dev2[:, :, :], dev[:, :, :], dev[:, :, :], ALU.mult))
            lk.link(nc.vector.tensor_tensor(dev[:, :, :], dev2[:, :, :], stT[:, 1], ALU.add))
            lk.link(nc.vector.tensor_reduce(gvar[:, :], dev[:, :, :], AX.X, ALU.add))
            nc.vector.tensor_scalar(gvar_eps[:, :], gvar[:, :], 0.25, GN_EPS, ALU.mult,
                                    ALU.add).then_inc(s.var_ready, 1)

        def inverse_std(pool, s, n):
            pool.wait_ge(s.var_ready, n + 1)
            nc.gpsimd.tensor_tensor(rstd[:, :], gvar_eps[:, :], minus_half[:, :], ALU.pow).then_inc(s.rstd_ready, 1)

        def norm_columns(dve, s, n, lk):
            lk.inc(nc.vector.tensor_copy(back[:, 0], gmean[:, :].unsqueeze(2).to_broadcast([P, GROUPS_PER_32, 4])))
            dve.wait_ge(s.rstd_ready, n + 1)
            lk.link(nc.vector.tensor_copy(back[:, 1], rstd[:, :].unsqueeze(2).to_broadcast([P, GROUPS_PER_32, 4])))
            lk.link(nc.vector.transpose(norm[:, :, :].rearrange("p a b -> p (a b)"),
                                        back[:, :, :, :].rearrange("p a g f -> p (a g f)")))

        def normalise(dve, s, n, q, h):
            if h > 0:
                dve.wait_ge(s.xlo_ready, HALVES * n + h)
            nc.vector.tensor_scalar(xn[:, :, :], x_raw[:, q, :, half(h)], norm[:, 0, 0:1], norm[:, 1, 0:1],
                                    ALU.subtract, ALU.mult).then_inc(s.xn_ready, 1)

        def split_x_hi(act, s, n, q, h):
            act.wait_ge(s.xn_ready, HALVES * n + h + 1)
            nc.scalar.copy(x_hi[:, q, h], xn[:, :, :]).then_inc(s.xhi_ready, 1)

        def split_x_lo(dve, s, n, q, h):
            dve.wait_ge(s.xhi_ready, HALVES * n + h + 1)
            nc.vector.tensor_tensor(x_lo[:, q, h], xn[:, :, :], x_hi[:, q, h].bitcast(f32),
                                    ALU.subtract).then_inc(s.xlo_ready, 1)

        def gate_product(pe, s, n, q, h):
            pe.wait_ge(s.xlo_ready, HALVES * n + h + 1)
            if h > 0:
                pe.wait_ge(s.gate_copied, HALVES * n + h)
            for j in range(NJ):
                w = gw[:, j].rearrange("p a e -> p (a e)")
                nc.tensor.matmul(g_ps[0:2 * E, 0:T], w, x_lo[:, q, h, j], start=(j == 0), stop=False)
                ins = nc.tensor.matmul(g_ps[0:2 * E, 0:T], w, x_hi[:, q, h, j], start=False, stop=(j == NJ - 1))
            ins.then_inc(s.gate_ready, 1)

        def gate_copy(act, s, n, h):
            act.wait_ge(s.gate_ready, HALVES * n + h + 1)
            nc.scalar.copy(lg_rows[:, h], g_ps[0:2 * E, 0:T]).then_inc(s.gate_copied, 1)

        def gate_move(sp, s, n):
            sp.wait_ge(s.gate_copied, HALVES * (n + 1))
            sp.dma_start(lg_dram, lg_rows[:, :, :].rearrange("r h t -> r (h t)")).then_inc(s.gate_written, 16)
            sp.wait_ge(s.gate_written, 16 * (n + 1))
            sp.dma_start(lg_pix[:, :, :], lg_dram.rearrange("r (p j) -> p r j", j=GJ)).then_inc(s.gate_moved, 16)

        def over_experts(ap):
            return ap.unsqueeze(1).to_broadcast([GP, E, GJ])

        def over_pixels(ap):
            return ap.unsqueeze(2).to_broadcast([GP, E, GJ])

        def gate_logits(dve, s, n, lk):
            dve.wait_ge(s.gate_moved, 16 * (n + 1))
            lk.link(nc.vector.tensor_tensor(lg[:, :, :], lg_pix[:, 0:E], lg_pix[:, E:2 * E], ALU.add))
            lk.link(nc.vector.tensor_tensor(lg[:, :, :], lg[:, :, :], over_pixels(gb[:, :]), ALU.add))
            lk.link(nc.vector.tensor_reduce(lg_max[:, :], lg[:, :, :].rearrange("p e j -> p j e"), AX.X, ALU.max))
            nc.vector.tensor_tensor(lg[:, :, :], lg[:, :, :], over_experts(lg_max[:, :]),
                                    ALU.subtract).then_inc(s.logit_ready, 1)

        def gate_exp(act, s, n):
            act.wait_ge(s.logit_ready, n + 1)
            nc.scalar.activation(ex[:, :, :], lg[:, :, :], ACT.Exp).then_inc(s.exp_ready, 1)

        def gate_top2(dve, s, n, lk):
            dve.wait_ge(s.exp_ready, n + 1)
            lk.link(nc.vector.tensor_reduce(ssum[:, :], ex[:, :, :].rearrange("p e j -> p j e"), AX.X, ALU.add))
            lk.link(nc.vector.reciprocal(lg_max[:, :], ssum[:, :]))
            lk.link(nc.vector.tensor_tensor(score[:, :, :], ex[:, :, :], over_experts(lg_max[:, :]), ALU.mult))
            lk.inc(nc.vector.tensor_tensor(pair_hi[:, :, :], score[:, 0:2], score[:, 2:4], ALU.max))
            lk.link(nc.vector.tensor_tensor(pair_lo[:, :, :], score[:, 0:2], score[:, 2:4], ALU.min))
            lk.inc(nc.vector.tensor_tensor(top1[:, :], pair_hi[:, 0], pair_hi[:, 1], ALU.max))
            lk.inc(nc.vector.tensor_tensor(mid[:, 0], pair_hi[:, 0], pair_hi[:, 1], ALU.min))
            lk.link(nc.vector.tensor_tensor(mid[:, 1], pair_lo[:, 0], pair_lo[:, 1], ALU.max))
            lk.link(nc.vector.tensor_tensor(top2[:, :], mid[:, 0], mid[:, 1], ALU.max))

        def gate_gap(dve):
            nc.vector.tensor_tensor(gap[:, :], top2[:, :], top1[:, :], ALU.subtract).then_inc(gap_ready, 1)

        def gate_gap_exp(act, n):
            act.wait_ge(gap_ready, n + 1)
            nc.scalar.activation(zexp[:, :], gap[:, :], ACT.Exp).then_inc(gexp_ready, 1)

        def gate_weights(dve, n, lk):
            dve.wait_ge(gexp_ready, n + 1)
            lk.link(nc.vector.tensor_scalar(den[:, :], zexp[:, :], 1.0, None, ALU.add))
            lk.link(nc.vector.reciprocal(wrow[:, 0], den[:, :]))
            lk.link(nc.vector.tensor_tensor(wrow[:, 1], zexp[:, :], wrow[:, 0], ALU.mult))
            lk.inc(nc.vector.tensor_tensor(wrow[:, 2:2 + E], over_pixels(present[0:GP, 0:E]),
                                           over_experts(wrow[:, 0]), ALU.mult))
            lk.link(nc.vector.tensor_tensor(wtmp[:, :, :], over_pixels(present[0:GP, E:2 * E]),
                                            over_experts(wrow[:, 1]), ALU.mult))
            lk.inc(nc.vector.tensor_tensor(wrow[:, 2:2 + E], wrow[:, 2:2 + E], wtmp[:, :, :], ALU.add))

        def count_picks(dve, lk):
            for rank, (sc, top) in enumerate(((score, top1), (rest, top2))):
                lk.link(nc.vector.tensor_tensor(pick[:, :, :], sc[:, :, :], over_experts(top[:, :]), ALU.is_equal))
                lk.link(nc.vector.tensor_tensor(pick[:, :, :], pick[:, :, :], over_pixels(order[:, :]), ALU.mult))
                lk.link(nc.vector.tensor_reduce(pick_max[:, :], pick[:, :, :].rearrange("p e j -> p j e"),
                                                AX.X, ALU.max))
                lk.link(nc.vector.tensor_tensor(onehot[:, rank], pick[:, :, :], over_experts(pick_max[:, :]),
                                                ALU.is_equal))
                if rank == 0:
                    lk.link(nc.vector.scalar_tensor_tensor(
                        rest[:, :, :].rearrange("p e j -> p (e j)"), onehot[:, 0].rearrange("p e j -> p (e j)"),
                        -2.0, score[:, :, :].rearrange("p e j -> p (e j)"), ALU.mult, ALU.add))
            lk.link(nc.vector.tensor_reduce(cnt_img[:, :], onehot[:, :, :, :].rearrange("p r e j -> p (r e) j"),
                                            AX.X, ALU.add))

        def sum_counts(pe, s):
            pe.wait_ge(s.cnt_ready, 1)
            nc.tensor.matmul(g_ps[:, 0:2 * E], ones[:, :], cnt[:, :], start=True, stop=True).then_inc(s.cnt_summed, 1)

        def find_present(dve, s, lk):
            dve.wait_ge(s.cnt_summed, 1)
            lk.link(nc.vector.tensor_scalar(present[:, :], g_ps[:, 0:2 * E], 0.5, None, ALU.is_gt))


        def mm1(pe, b, par, u, first=False):
            h, e = divmod(u, E)
            if first:
                pe.wait_ge(wlo_ready, 2)
            elif isinstance(b, int) and b == 0 and h == 0:
                pe.wait_ge(wlo_ready, 2 + e)
            for k in range(NK):
                if not first:
                    pe.wait_ge(relu_done, CHUNKS * b + NK * u + k - (ZB - 1))
                z = z_ps[:, (NK * u + k) % ZB, 0:T]
                ks = slice(k * P, (k + 1) * P)
                for j in range(NJ):
                    hi, lo = x_hi[:, par, h, j], x_lo[:, par, h, j]
                    nc.tensor.matmul(z, w1_hi[:, e, j, ks], lo, start=(j == 0), stop=False)
                    nc.tensor.matmul(z, w1_lo[:, e, j, ks], hi, start=False, stop=False)
                    ins = nc.tensor.matmul(z, w1_hi[:, e, j, ks], hi, start=False, stop=(j == NJ - 1))
                ins.then_inc(z_ready, 1)

        def mm2(pe, b, u):
            h, e = divmod(u, E)
            if isinstance(b, int) and b == 0 and h == 0:
                pe.wait_ge(wlo_ready, 2 + E + e)
            if e == 0:
                pe.wait_ge(out_ready, HALVES * b + h)
            for k in range(NK):
                slot = (NK * u + k) % RING
                pe.wait_ge(hlo_ready, CHUNKS * b + NK * u + k + 1)
                for m in range(NJ):
                    y = y_ps[:, m, 0:T]
                    ms = slice(m * P, (m + 1) * P)
                    first, last = e == 0 and k == 0, e == E - 1 and k == NK - 1
                    nc.tensor.matmul(y, w2_hi[:, e, k, ms], h_lo[:, slot], start=first, stop=False)
                    nc.tensor.matmul(y, w2_lo[:, e, k, ms], h_hi[:, slot], start=False, stop=False)
                    ins = nc.tensor.matmul(y, w2_hi[:, e, k, ms], h_hi[:, slot], start=False, stop=last)
            ins.then_inc(unit_done, 1)

        def relu(act, b, q):
            e = (q // NK) % E
            act.wait_ge(z_ready, CHUNKS * b + q + 1)
            nc.scalar.activation(hid[:, q % RING], z_ps[:, q % ZB, 0:T], ACT.Relu,
                                 bias=b1_sb[:, e, q % NK:q % NK + 1]).then_inc(relu_done, 1)

        def split_h_hi(act, b, q):
            act.wait_ge(scaled, CHUNKS * b + q + 1)
            nc.scalar.copy(h_hi[:, q % RING], hid[:, q % RING]).then_inc(hhi_ready, 1)

        def scale(dve, b, par, q):
            img = q // CHUNKS
            u = (q % CHUNKS) // NK
            h, e = divmod(u, E)
            if e == 0 and q % NK == 0:
                dve.wait_ge(rows_loaded[h], 16 * (b + img + 1))
            dve.wait_ge(relu_done, CHUNKS * b + q + 1)
            nc.vector.tensor_tensor(hid[:, q % RING], hid[:, q % RING], rows[:, (par + img) % 2, h, 2 + e],
                                    ALU.mult).then_inc(scaled, 1)

        def split_h_lo(dve, b, q):
            dve.wait_ge(hhi_ready, CHUNKS * b + q + 1)
            nc.vector.tensor_tensor(h_lo[:, q % RING], hid[:, q % RING], h_hi[:, q % RING].bitcast(f32),
                                    ALU.subtract).then_inc(hlo_ready, 1)

        def add_bias(dve, par, h, rank, lk):
            for m in range(NJ):
                xs = x_raw[:, par, m, half(h)]
                lk.inc(nc.vector.scalar_tensor_tensor(xs, rows[:, par, h, rank], bias01[:, rank, m:m + 1], xs,
                                                      ALU.mult, ALU.add))

        def add_product(dve, b, par, h):
            dve.wait_ge(unit_done, UNITS * b + E * (h + 1))
            xs = x_raw[:, par, :, half(h)]
            nc.vector.tensor_tensor(xs, xs, y_ps[:, :, 0:T], ALU.add).then_inc(out_ready, 1)

        def store(sp, b, par, h):
            sp.wait_ge(out_ready, HALVES * b + h + 1)
            sp.dma_start(out_v[b][:, :, half(h)], x_raw[:, par, :, half(h)]).then_inc(stored, 16)

        def rows_out(sp, n, q, lk_value):
            sp.wait_ge(dve_step, lk_value)
            sp.dma_start(rows_dram[q].rearrange("r (p j) -> p r j", j=GJ), wrow[:, :, :]).then_inc(rows_written, 16)
            sp.wait_ge(rows_written, 16 * (n + 1))
            for h in range(HALVES):
                sp.dma_start(rows[:, q, h],
                             rows_dram[q][:, half(h)].unsqueeze(0).to_broadcast([P, ROWS, T])
                             ).then_inc(rows_loaded[h], 16)

        def each_image(eng, image):
            image(0, 0, True, False)
            with eng.Fori(0, (B - 2) // 2) as i:
                image(i * 2 + 1, 1, False, False)
                image(i * 2 + 2, 0, False, False)
            image(B - 1, (B - 1) % 2, False, True)

        START_LINKS = {}

        block = ctx.enter_context(nc.Block())

        @block.vector
        def _(dve):
            lk = Links(dve, dve_step, 0)
            nc.vector.memset(st[:, :, :], 1.0)
            nc.vector.memset(minus_half[:, :], -0.5)
            nc.vector.memset(ones[:, :], 1.0)
            for e in range(E):
                ins = nc.vector.memset(order[:, e:e + 1], float(E - e))
            ins.then_inc(const_ready, 1)
            dve.wait_ge(const_ready, 1)

            stats_first(dve, main, 0, 0)
            stats_rest(dve, main, 0, 0, lk)
            group_stats(dve, main, 0, lk)
            dve.wait_ge(whi_ready, 1)
            nc.vector.tensor_tensor(gw[:, :, 1], gw_in[:, :, :], gw[:, :, 0].bitcast(f32),
                                    ALU.subtract).then_inc(wlo_ready, 1)
            norm_columns(dve, main, 0, lk)
            for h in range(HALVES):
                normalise(dve, main, 0, 0, h)
                split_x_lo(dve, main, 0, 0, h)

            def weight_lo(which, e):
                src, hi, lo = ((w1_in, w1_hi, w1_lo), (w2_in, w2_hi, w2_lo))[which]
                w = NJ * HID
                dve.wait_ge(whi_ready, 2 + E * which + e)
                nc.vector.tensor_tensor(lo[:, e].rearrange("p j d -> p (j d)"), src[:, e * w:(e + 1) * w],
                                        hi[:, e].rearrange("p j d -> p (j d)").bitcast(f32),
                                        ALU.subtract).then_inc(wlo_ready, 1)

            weight_lo(0, 0)
            dve.wait_ge(small_loaded, 64)
            gate_logits(dve, main, 0, lk)
            gate_top2(dve, main, 0, lk)
            gate_gap(dve)
            count_picks(dve, lk)
            nc.vector.tensor_copy(cnt[:, :], cnt_img[:, :]).then_inc(main.cnt_ready, 1)
            find_present(dve, main, lk)
            lk.link(nc.vector.tensor_reduce(fewest[:, :], present[:, :], AX.X, ALU.min))
            nc.vector.tensor_scalar(missing[:, :], fewest[:, :], -1.0, 1.0, ALU.mult, ALU.add).then_inc(flag_ready, 1)
            for e in range(1, E):
                weight_lo(0, e)
            for e in range(E):
                weight_lo(1, e)
            dve.wait_ge(flag_ready, 1)
            flag = dve.value_load(missing[0:1, 0:1], min_val=0, max_val=1)
            with dve.If(flag > 0):
                nc.vector.memset(pad[:, :], 0.0).then_inc(scan_free, 1)
                with dve.Fori(1, B) as b:
                    n = b - 1
                    sk = Links(dve, scan_step, n * SCAN_LINKS)
                    stats_first(dve, scan, n, 1)
                    stats_rest(dve, scan, n, 1, sk)
                    group_stats(dve, scan, n, sk)
                    norm_columns(dve, scan, n, sk)
                    for h in range(HALVES):
                        normalise(dve, scan, n, 1, h)
                        split_x_lo(dve, scan, n, 1, h)
                    gate_logits(dve, scan, n, sk)
                    gate_top2(dve, scan, n, sk)
                    count_picks(dve, sk)
                    nc.vector.tensor_tensor(cnt[:, :], cnt[:, :], cnt_img[:, :], ALU.add).then_inc(scan_free, 1)
                    assert sk.n == SCAN_LINKS, sk.n
                dve.wait_ge(scan_free, B)
                nc.vector.tensor_copy(cnt_img[:, :], cnt[:, :]).then_inc(scan.cnt_ready, 1)
                sk = Links(dve, scan_step, (B - 1) * SCAN_LINKS)
                find_present(dve, scan, sk)

            for rank in range(2):
                lk.link(nc.vector.tensor_scalar(bias01[:, rank], b2_sb[:, 0], present[:, E * rank:E * rank + 1],
                                                None, ALU.mult))
            for e in range(1, E):
                for rank in range(2):
                    ins = nc.vector.scalar_tensor_tensor(
                        bias01[:, rank], b2_sb[:, e], present[:, E * rank + e:E * rank + e + 1],
                        bias01[:, rank], ALU.mult, ALU.add)
                    lk.inc(ins)
                lk.wait()
            gate_weights(dve, 0, lk)
            START_LINKS["n"] = lk.n
            scale(dve, 0, 0, 0)

            def image(b, par, first, last):
                nxt = 1 - par
                n = b + 1
                lk = Links(dve, dve_step, DVE_LINKS * b + START_LINKS["n"])
                for q in range(CHUNKS):
                    if q == NK - 1 and not first:
                        add_product(dve, b - 1, nxt, 1)
                    if q == E * NK + NK - 1:
                        add_product(dve, b, par, 0)
                    if not (last and q == CHUNKS - 1):
                        scale(dve, b, par, q + 1)
                    split_h_lo(dve, b, q)
                    if q in (7, 9):
                        add_bias(dve, par, 0, (q - 7) // 2, lk)
                        lk.wait()
                    if q in (19, 21):
                        add_bias(dve, par, 1, (q - 19) // 2, lk)
                        lk.wait()
                    if last:
                        continue
                    if q == 4:
                        stats_first(dve, main, n, nxt)
                    if q == 5:
                        stats_rest(dve, main, n, nxt, lk)
                    if q == 6:
                        group_stats(dve, main, n, lk)
                    if q == 8:
                        norm_columns(dve, main, n, lk)
                        normalise(dve, main, n, nxt, 0)
                    if q == 10:
                        split_x_lo(dve, main, n, nxt, 0)
                        normalise(dve, main, n, nxt, 1)
                    if q == 12:
                        split_x_lo(dve, main, n, nxt, 1)
                    if q == 16:
                        gate_logits(dve, main, n, lk)
                    if q == 17:
                        gate_top2(dve, main, n, lk)
                        gate_gap(dve)
                    if q == 18:
                        gate_weights(dve, n, lk)
                        START_LINKS["rows"] = lk.n
                if not last:
                    assert lk.n == DVE_LINKS, lk.n
                else:
                    add_product(dve, b, par, 1)

            each_image(dve, image)

        @block.scalar
        def _(act):
            def weight_hi(which, e):
                src, hi, loaded = ((w1_in, w1_hi, w1_loaded), (w2_in, w2_hi, w2_loaded))[which]
                w = NJ * HID
                act.wait_ge(loaded[e], 16)
                nc.scalar.copy(hi[:, e].rearrange("p j d -> p (j d)"), src[:, e * w:(e + 1) * w]).then_inc(whi_ready, 1)

            act.wait_ge(small_loaded, 64)
            nc.scalar.copy(gw[:, :, 0], gw_in[:, :, :]).then_inc(whi_ready, 1)
            weight_hi(0, 0)
            for h in range(HALVES):
                split_x_hi(act, main, 0, 0, h)
            for h in range(HALVES):
                gate_copy(act, main, 0, h)
            gate_exp(act, main, 0)
            gate_gap_exp(act, 0)
            for e in range(1, E):
                weight_hi(0, e)
            for e in range(E):
                weight_hi(1, e)
            act.wait_ge(flag_ready, 1)
            flag = act.value_load(missing[0:1, 0:1], min_val=0, max_val=1)
            with act.If(flag > 0):
                with act.Fori(1, B) as b:
                    n = b - 1
                    for h in range(HALVES):
                        split_x_hi(act, scan, n, 1, h)
                    for h in range(HALVES):
                        gate_copy(act, scan, n, h)
                    gate_exp(act, scan, n)
            relu(act, 0, 0)

            def image(b, par, first, last):
                nxt = 1 - par
                n = b + 1
                for q in range(CHUNKS):
                    if not (last and q == CHUNKS - 1):
                        relu(act, b, q + 1)
                    split_h_hi(act, b, q)
                    if last:
                        continue
                    if q == 9:
                        split_x_hi(act, main, n, nxt, 0)
                    if q == 11:
                        split_x_hi(act, main, n, nxt, 1)
                    if q == 12:
                        gate_copy(act, main, n, 0)
                    if q == 13:
                        gate_copy(act, main, n, 1)
                    if q == 16:
                        gate_exp(act, main, n)
                    if q == 17:
                        gate_gap_exp(act, n)

            each_image(act, image)

        @block.gpsimd
        def _(pool):
            pool.wait_ge(const_ready, 1)
            inverse_std(pool, main, 0)
            pool.wait_ge(flag_ready, 1)
            flag = pool.value_load(missing[0:1, 0:1], min_val=0, max_val=1)
            with pool.If(flag > 0):
                with pool.Fori(1, B) as b:
                    inverse_std(pool, scan, b - 1)
            with pool.Fori(1, B) as b:
                inverse_std(pool, main, b)

        @block.sync
        def _(sp):
            load_x(sp, main, 0, 0)
            sp.dma_start(gw_in[:, :, :], gate_w.rearrange("(p j) e -> p j e", j=NJ)).then_inc(small_loaded, 16)
            sp.dma_start(gb[:, :], gate_b.unsqueeze(0).to_broadcast([GP, E])).then_inc(small_loaded, 16)
            sp.dma_start(b1_sb[:, :, :], b1).then_inc(small_loaded, 16)
            sp.dma_start(b2_sb[:, :, :], b2).then_inc(small_loaded, 16)
            for src, dst, loaded in ((w1, w1_in, w1_loaded), (w2, w2_in, w2_loaded)):
                w = NJ * HID
                for e in range(E):
                    sp.dma_start(dst[:, e * w:(e + 1) * w], src[:, e]).then_inc(loaded[e], 16)
            gate_move(sp, main, 0)
            sp.wait_ge(flag_ready, 1)
            flag = sp.value_load(missing[0:1, 0:1], min_val=0, max_val=1)
            with sp.If(flag > 0):
                with sp.Fori(1, B) as b:
                    sp.wait_ge(scan_free, b)
                    load_x(sp, scan, b, 1)
                    gate_move(sp, scan, b - 1)
            sp.wait_ge(wlo_ready, 1 + 2 * E)
            rows_out(sp, 0, 0, START_LINKS["n"])

            def image(b, par, first, last):
                nxt = 1 - par
                n = b + 1
                if not first:
                    store(sp, b - 1, nxt, 1)
                if not last:
                    if not first:
                        sp.wait_ge(stored, 16 * HALVES * b)
                    load_x(sp, main, n, nxt)
                    gate_move(sp, main, n)
                store(sp, b, par, 0)
                if not last:
                    rows_out(sp, n, nxt, DVE_LINKS * b + START_LINKS["n"] + START_LINKS["rows"])

            each_image(sp, image)
            store(sp, B - 1, (B - 1) % 2, 1)
            sp.wait_ge(stored, 16 * HALVES * B)

        @block.tensor
        def _(pe):
            pe.wait_ge(wlo_ready, 1)
            for h in range(HALVES):
                gate_product(pe, main, 0, 0, h)
            mm1(pe, 0, 0, 0, first=True)
            pe.wait_ge(const_ready, 1)
            sum_counts(pe, main)
            pe.wait_ge(flag_ready, 1)
            flag = pe.value_load(missing[0:1, 0:1], min_val=0, max_val=1)
            with pe.If(flag > 0):
                with pe.Fori(1, B) as b:
                    for h in range(HALVES):
                        gate_product(pe, scan, b - 1, 1, h)
                sum_counts(pe, scan)

            def image(b, par, first, last):
                nxt = 1 - par
                n = b + 1
                for u in range(UNITS):
                    if u == 4 and not last:
                        gate_product(pe, main, n, nxt, 0)
                    if u < UNITS - 1:
                        mm1(pe, b, par, u + 1)
                    elif not last:
                        mm1(pe, b + 1, nxt, 0)
                    if u == 4 and not last:
                        gate_product(pe, main, n, nxt, 1)
                    mm2(pe, b, u)

            each_image(pe, image)




def kernel(x, L0_conv_gate_w, L0_conv_gate_b, L0_conv_w1, L0_conv_b1, L0_conv_w2, L0_conv_b2):
    import numpy as np
    import concourse.bacc as bacc
    from concourse.bass_utils import run_bass_kernel_spmd

    w1 = np.asarray(L0_conv_w1).reshape(E, HID, P, NJ).transpose(2, 0, 3, 1)
    w2 = np.asarray(L0_conv_w2).reshape(E, P, NJ, NK, P).transpose(4, 0, 3, 2, 1).reshape(P, E, NK, C)
    b1 = np.asarray(L0_conv_b1).reshape(E, NK, P).transpose(2, 0, 1)
    b2 = np.asarray(L0_conv_b2).reshape(E, P, NJ).transpose(1, 0, 2)
    arrays = {"x": x, "gate_w": L0_conv_gate_w, "gate_b": L0_conv_gate_b, "w1": w1, "b1": b1, "w2": w2, "b2": b2}
    arrays = {f"in_{k}": np.ascontiguousarray(v) for k, v in arrays.items()}

    nc = bacc.Bacc("TRN2", target_bir_lowering=False, num_devices=1)
    args = [nc.dram_tensor(k, v.shape, mybir.dt.from_np(v.dtype), kind="ExternalInput").ap()
            for k, v in arrays.items()]
    out = nc.dram_tensor("out", arrays["in_x"].shape, mybir.dt.float32, kind="ExternalOutput").ap()
    conv_moe(nc, *args, out)
    r = run_bass_kernel_spmd(nc, [arrays], core_ids=[0])
    return r.results[0]["out"]
```

```python
import concourse.bass as bass
from concourse import mybir
from contextlib import ExitStack

B, C, PIX = 32, 384, 784
E, HID = 4, 384
P = 128
NJ = C // P
NK = HID // P
HALVES = 2
T = PIX // HALVES
GROUPS_PER_32 = 8
GN_EPS = 1e-5
QUART = PIX // 4
GJ = -(-QUART // 32)
PARTS = 3
ROWS = 2 + E
UNITS = HALVES * E
CHUNKS = UNITS * NK
ZB = 4
RING = 2 * NK
WARM = 8
AHEAD = 2
DVE_LINKS = 45
SCAN_LINKS = 38


def conv_moe(nc, x, gate_w, gate_b, w1, b1, w2, b2, out):
    f32, f32r, bf16, i32 = mybir.dt.float32, mybir.dt.float32r, mybir.dt.bfloat16, mybir.dt.int32
    ALU, ACT, AX = mybir.AluOpType, mybir.ActivationFunctionType, mybir.AxisListType

    x_v = x.rearrange("b (p j) h w -> b p j (h w)", j=NJ)
    out_v = out.rearrange("b (p j) h w -> b p j (h w)", j=NJ)

    ctx = ExitStack()
    with ctx:
        def sb(name, shape, dt=f32):
            return ctx.enter_context(nc.sbuf_tensor(name, shape, dt))

        def pb(name, shape):
            return ctx.enter_context(nc.psum_tensor(name, shape, f32))

        def sem(name):
            return ctx.enter_context(nc.semaphore(name))

        w1_hi = sb("w1_hi", [P, E, NJ, HID], f32r)
        w1_lo = sb("w1_lo", [P, E, NJ, HID], f32r)
        w2_hi = sb("w2_hi", [P, E, NK, C], f32r)
        w2_lo = sb("w2_lo", [P, E, NK, C], f32r)
        gw_in = sb("gw_in", [P, NJ, E])
        gw_part = sb("gw_part", [P, NJ, 32], bf16)
        gw_rest = sb("gw_rest", [P, 2, NJ, E])
        gb = sb("gb", [P, E])
        b1_sb = sb("b1_sb", [P, E, NK])
        b2_sb = sb("b2_sb", [P, E, NJ])

        x_raw = sb("x_raw", [P, 2, NJ, PIX])
        x_hi = sb("x_hi", [P, 2, HALVES, NJ, T], f32r)
        x_lo = sb("x_lo", [P, 2, HALVES, NJ, T], f32r)
        x_part = sb("x_part", [P, PARTS, HALVES, NJ, T], bf16)
        xn = sb("xn", [P, NJ, T])
        xn_rest = sb("xn_rest", [P, NJ, T])
        rows = sb("rows", [P, HALVES, ROWS, T])
        hid = sb("hid", [P, RING, T])
        slab = NJ * HID
        w1_in = [rows[:, :, :, :].rearrange("p h r t -> p (h r t)")[:, e * slab:(e + 1) * slab] for e in range(E)]
        w2_in = [x_raw[:, 1].rearrange("p j t -> p (j t)")[:, (e % 2) * slab:(e % 2 + 1) * slab] for e in range(E)]
        h_hi = sb("h_hi", [P, RING, T], f32r)
        h_lo = sb("h_lo", [P, RING, T], f32r)

        st6 = sb("st6", [P, NJ * HALVES, 6])
        st = sb("st", [P, 2, 32])
        stT = sb("stT", [P, 2, GROUPS_PER_32, 4])
        pad = sb("pad", [1, 1])
        gsum = sb("gsum", [P, GROUPS_PER_32])
        gmean = sb("gmean", [P, GROUPS_PER_32])
        dev = sb("dev", [P, GROUPS_PER_32, 4])
        dev2 = sb("dev2", [P, GROUPS_PER_32, 4])
        gvar = sb("gvar", [P, GROUPS_PER_32])
        gvar_eps = sb("gvar_eps", [P, GROUPS_PER_32])
        minus_half = sb("minus_half", [P, GROUPS_PER_32])
        rstd = sb("rstd", [P, GROUPS_PER_32])
        back = sb("back", [P, 2, GROUPS_PER_32, 4])
        norm = sb("norm", [P, 2, 32])

        lg_rows = sb("lg_rows", [P, GJ * 32])
        lg_pix = sb("lg_pix", [P, GJ, 32])
        lg = sb("lg", [P, GJ, E])
        lg_max = sb("lg_max", [P, GJ])
        ex = sb("ex", [P, GJ, E])
        ssum = sb("ssum", [P, GJ])
        score = sb("score", [P, GJ, E])
        pair_hi = sb("pair_hi", [P, GJ, 2])
        pair_lo = sb("pair_lo", [P, GJ, 2])
        top1 = sb("top1", [P, GJ])
        top2 = sb("top2", [P, GJ])
        mid = sb("mid", [P, 2, GJ])
        gap = sb("gap", [P, GJ])
        zexp = sb("zexp", [P, GJ])
        den = sb("den", [P, GJ])
        wpix = sb("wpix", [P, GJ, 32])
        wrow = sb("wrow", [P, GJ * 32])
        wtmp = sb("wtmp", [P, GJ, E])
        order = sb("order", [P, E])
        valid = sb("valid", [P, GJ])
        pick = sb("pick", [P, GJ, E])
        pick_max = sb("pick_max", [P, GJ])
        onehot = sb("onehot", [P, 2, GJ, E])
        rest = sb("rest", [P, GJ, E])
        cnt = sb("cnt", [P, 2, E])
        cnt_img = sb("cnt_img", [P, 2, E])
        ones = sb("ones", [P, P])
        present = sb("present", [P, 2 * E])
        fewest = sb("fewest", [P, 1])
        missing = sb("missing", [P, 1], i32)
        bias01 = sb("bias01", [P, 2, NJ])

        y_ps = pb("y_ps", [P, NJ, 512])
        z_ps = pb("z_ps", [P, ZB, 512])
        g_ps = pb("g_ps", [P, 512])

        rows_dram = nc.dram_tensor("rows_dram", (32, PIX), f32).ap()

        small_loaded = sem("small_loaded")
        first_loaded = [sem(f"first_loaded{j}") for j in range(NJ)]
        w1_loaded = [sem(f"w1_loaded{e}") for e in range(E)]
        w2_loaded = [sem(f"w2_loaded{e}") for e in range(E)]
        whi_ready = sem("whi_ready")
        wlo_ready = sem("wlo_ready")
        gw_ready = sem("gw_ready")
        const_ready = sem("const_ready")
        dve_step = sem("dve_step")
        flag_ready = sem("flag_ready")
        present_ready = sem("present_ready")
        z_ready = sem("z_ready")
        relu_done = sem("relu_done")
        scaled = sem("scaled")
        hhi_ready = sem("hhi_ready")
        hlo_ready = sem("hlo_ready")
        unit_done = sem("unit_done")
        out_ready = sem("out_ready")
        tail_product = sem("tail_product")
        tail_ready = sem("tail_ready")
        stored = sem("stored")
        rows_written = sem("rows_written")
        first_row_loaded = sem("first_row_loaded")
        rows_loaded = [sem("rows_loaded0"), sem("rows_loaded1")]
        gap_ready = sem("gap_ready")
        gexp_ready = sem("gexp_ready")

        class Sems:

            def __init__(self, pre):
                self.x_loaded = [sem(pre + f"x_loaded{h}") for h in range(HALVES)]
                self.var_ready = sem(pre + "var_ready")
                self.rstd_ready = sem(pre + "rstd_ready")
                self.xn_ready = sem(pre + "xn_ready")
                self.part1_ready = sem(pre + "part1_ready")
                self.rest_ready = sem(pre + "rest_ready")
                self.part2_ready = sem(pre + "part2_ready")
                self.part3_ready = sem(pre + "part3_ready")
                self.xhi_ready = sem(pre + "xhi_ready")
                self.xlo_ready = sem(pre + "xlo_ready")
                self.gate_ready = sem(pre + "gate_ready")
                self.gate_copied = sem(pre + "gate_copied")
                self.logit_ready = sem(pre + "logit_ready")
                self.exp_ready = sem(pre + "exp_ready")
                self.cnt_ready = sem(pre + "cnt_ready")
                self.cnt_summed = sem(pre + "cnt_summed")

        main = Sems("")
        scan = Sems("scan_")
        scan_step = sem("scan_step")
        scan_free = sem("scan_free")

        def half(h):
            return slice(h * T, (h + 1) * T)


        def load_x(sp, s, b, q, h):
            sp.dma_start(x_raw[:, q, :, half(h)], x_v[b][:, :, half(h)]).then_inc(s.x_loaded[h], 16)

        class Links:

            def __init__(self, eng, s, base):
                self.eng, self.s, self.base, self.n = eng, s, base, 0

            def inc(self, ins):
                self.n += 1
                ins.then_inc(self.s, 1)

            def wait(self):
                self.eng.wait_ge(self.s, self.base + self.n)

            def link(self, ins):
                self.inc(ins)
                self.wait()

        def stats(dve, s, loads, q, h, lk):
            dve.wait_ge(s.x_loaded[h], 16 * loads)
            for j in range(NJ):
                ins = nc.vector.bn_stats(st6[:, HALVES * j + h], x_raw[:, q, j, half(h)])
            lk.inc(ins)

        def group_stats(dve, s, n, lk):
            lk.wait()
            nc.vector.memset(pad[:, :], 0.0)
            lk.link(nc.vector.bn_aggr(st[:, :, 0], st6[:, :, :].rearrange("p a b -> p (a b)")))
            lk.link(nc.vector.transpose(stT[:, :, :, :].rearrange("p a g f -> p (a g f)"),
                                        st[:, :, :].rearrange("p a b -> p (a b)")))
            lk.link(nc.vector.tensor_reduce(gsum[:, :], stT[:, 0], AX.X, ALU.add))
            lk.link(nc.vector.tensor_scalar(gmean[:, :], gsum[:, :], 0.25, None, ALU.mult))
            lk.link(nc.vector.tensor_tensor(dev[:, :, :], stT[:, 0],
                                            gmean[:, :].unsqueeze(2).to_broadcast([P, GROUPS_PER_32, 4]),
                                            ALU.subtract))
            lk.link(nc.vector.tensor_tensor(dev2[:, :, :], dev[:, :, :], dev[:, :, :], ALU.mult))
            lk.link(nc.vector.tensor_tensor(dev[:, :, :], dev2[:, :, :], stT[:, 1], ALU.add))
            lk.link(nc.vector.tensor_reduce(gvar[:, :], dev[:, :, :], AX.X, ALU.add))
            nc.vector.tensor_scalar(gvar_eps[:, :], gvar[:, :], 0.25, GN_EPS, ALU.mult,
                                    ALU.add).then_inc(s.var_ready, 1)

        def inverse_std(pool, s, n):
            pool.wait_ge(s.var_ready, n + 1)
            nc.gpsimd.tensor_tensor(rstd[:, :], gvar_eps[:, :], minus_half[:, :], ALU.pow).then_inc(s.rstd_ready, 1)

        def norm_columns(dve, s, n, lk):
            lk.inc(nc.vector.tensor_copy(back[:, 0], gmean[:, :].unsqueeze(2).to_broadcast([P, GROUPS_PER_32, 4])))
            dve.wait_ge(s.rstd_ready, n + 1)
            lk.link(nc.vector.tensor_copy(back[:, 1], rstd[:, :].unsqueeze(2).to_broadcast([P, GROUPS_PER_32, 4])))
            lk.link(nc.vector.transpose(norm[:, :, :].rearrange("p a b -> p (a b)"),
                                        back[:, :, :, :].rearrange("p a g f -> p (a g f)")))

        xn_of = {True: (xn[:, :, :], hid[:, 0:NJ]), False: (xn[:, :, :], xn[:, :, :])}
        rest_of = {True: (xn_rest[:, :, :], hid[:, NJ:RING]), False: (xn_rest[:, :, :], xn_rest[:, :, :])}

        def normalise(dve, s, n, q, h, alone=False):
            nc.vector.tensor_scalar(xn_of[alone][h], x_raw[:, q, :, half(h)], norm[:, 0, 0:1], norm[:, 1, 0:1],
                                    ALU.subtract, ALU.mult).then_inc(s.xn_ready, 1)

        def part1(act, s, n, h, alone=False):
            act.wait_ge(s.xn_ready, HALVES * n + h + 1)
            nc.scalar.copy(x_part[:, 0, h], xn_of[alone][h]).then_inc(s.part1_ready, 1)

        def less_part1(dve, s, n, h, alone=False):
            dve.wait_ge(s.part1_ready, HALVES * n + h + 1)
            nc.vector.tensor_tensor(rest_of[alone][h], xn_of[alone][h], x_part[:, 0, h],
                                    ALU.subtract).then_inc(s.rest_ready, 1)

        def part2(act, s, n, h, alone=False):
            act.wait_ge(s.rest_ready, HALVES * n + h + 1)
            nc.scalar.copy(x_part[:, 1, h], rest_of[alone][h]).then_inc(s.part2_ready, 1)

        def part3(dve, s, n, h, alone=False):
            dve.wait_ge(s.part2_ready, HALVES * n + h + 1)
            nc.vector.tensor_tensor(x_part[:, 2, h], rest_of[alone][h], x_part[:, 1, h],
                                    ALU.subtract).then_inc(s.part3_ready, 1)

        def split_x_hi(act, s, n, q, h, alone=False):
            act.wait_ge(s.xn_ready, HALVES * n + h + 1)
            nc.scalar.copy(x_hi[:, q, h], xn_of[alone][h]).then_inc(s.xhi_ready, 1)

        def split_x_lo(dve, s, n, q, h, alone=False):
            dve.wait_ge(s.xhi_ready, HALVES * n + h + 1)
            nc.vector.tensor_tensor(x_lo[:, q, h], xn_of[alone][h], x_hi[:, q, h].bitcast(f32),
                                    ALU.subtract).then_inc(s.xlo_ready, 1)

        def gate_product(pe, s, n):
            pe.wait_ge(s.part3_ready, HALVES * (n + 1))
            for t in reversed(range(PARTS)):
                for j in range(NJ):
                    for g in range(4):
                        h, at = divmod(g * QUART, T)
                        ins = nc.tensor.matmul(g_ps[32 * g:32 * (g + 1), 0:QUART], gw_part[:, j],
                                               x_part[:, t, h, j, at:at + QUART],
                                               start=(t == PARTS - 1 and j == 0), stop=(t == 0 and j == NJ - 1),
                                               tile_position=(0, 32 * g))
            ins.then_inc(s.gate_ready, 1)

        def gate_copy(act, s, n):
            act.wait_ge(s.gate_ready, n + 1)
            nc.scalar.copy(lg_rows[:, 0:QUART], g_ps[:, 0:QUART]).then_inc(s.gate_copied, 1)

        def over_experts(ap):
            return ap.unsqueeze(2).to_broadcast([P, GJ, E])

        def over_pixels(ap):
            return ap.unsqueeze(1).to_broadcast([P, GJ, E])

        def gate_logits(dve, s, n, lk):
            dve.wait_ge(s.gate_copied, n + 1)
            lk.link(nc.vector.transpose(lg_pix[:, :, :].rearrange("p c r -> p (c r)"), lg_rows[:, :]))
            lk.link(nc.vector.tensor_reduce(
                lg[:, :, :], lg_pix[:, :, 0:PARTS * E].rearrange("p c (t e) -> p c e t", e=E), AX.X, ALU.add))
            lk.link(nc.vector.tensor_tensor(lg[:, :, :], lg[:, :, :], over_pixels(gb[:, :]), ALU.add))
            lk.link(nc.vector.tensor_reduce(lg_max[:, :], lg[:, :, :], AX.X, ALU.max))
            nc.vector.tensor_tensor(lg[:, :, :], lg[:, :, :], over_experts(lg_max[:, :]),
                                    ALU.subtract).then_inc(s.logit_ready, 1)

        def gate_exp(act, s, n):
            act.wait_ge(s.logit_ready, n + 1)
            nc.scalar.activation(ex[:, :, :], lg[:, :, :], ACT.Exp).then_inc(s.exp_ready, 1)

        def gate_top2(dve, s, n, lk):
            dve.wait_ge(s.exp_ready, n + 1)
            lk.link(nc.vector.tensor_reduce(ssum[:, :], ex[:, :, :], AX.X, ALU.add))
            lk.link(nc.vector.reciprocal(lg_max[:, :], ssum[:, :]))
            lk.link(nc.vector.tensor_tensor(score[:, :, :], ex[:, :, :], over_experts(lg_max[:, :]), ALU.mult))
            lk.inc(nc.vector.tensor_tensor(pair_hi[:, :, :], score[:, :, 0:2], score[:, :, 2:4], ALU.max))
            lk.link(nc.vector.tensor_tensor(pair_lo[:, :, :], score[:, :, 0:2], score[:, :, 2:4], ALU.min))
            lk.inc(nc.vector.tensor_tensor(top1[:, :], pair_hi[:, :, 0], pair_hi[:, :, 1], ALU.max))
            lk.inc(nc.vector.tensor_tensor(mid[:, 0], pair_hi[:, :, 0], pair_hi[:, :, 1], ALU.min))
            lk.link(nc.vector.tensor_tensor(mid[:, 1], pair_lo[:, :, 0], pair_lo[:, :, 1], ALU.max))
            lk.link(nc.vector.tensor_tensor(top2[:, :], mid[:, 0], mid[:, 1], ALU.max))

        def gate_gap(dve):
            nc.vector.tensor_tensor(gap[:, :], top2[:, :], top1[:, :], ALU.subtract).then_inc(gap_ready, 1)

        def gate_gap_exp(act, n):
            act.wait_ge(gap_ready, n + 1)
            nc.scalar.activation(zexp[:, :], gap[:, :], ACT.Exp).then_inc(gexp_ready, 1)

        def gate_weights(dve, n, lk):
            dve.wait_ge(gexp_ready, n + 1)
            lk.link(nc.vector.tensor_scalar(den[:, :], zexp[:, :], 1.0, None, ALU.add))
            lk.link(nc.vector.reciprocal(wpix[:, :, E], den[:, :]))
            lk.link(nc.vector.tensor_tensor(wpix[:, :, E + 1], zexp[:, :], wpix[:, :, E], ALU.mult))

        def gate_coefs(lk):
            lk.inc(nc.vector.tensor_tensor(wpix[:, :, 0:E], over_pixels(present[:, 0:E]),
                                           over_experts(wpix[:, :, E]), ALU.mult))
            lk.link(nc.vector.tensor_tensor(wtmp[:, :, :], over_pixels(present[:, E:2 * E]),
                                            over_experts(wpix[:, :, E + 1]), ALU.mult))
            lk.link(nc.vector.tensor_tensor(wpix[:, :, 0:E], wpix[:, :, 0:E], wtmp[:, :, :], ALU.add))
            lk.inc(nc.vector.transpose(wrow[:, :], wpix[:, :, :].rearrange("p c r -> p (c r)")))

        def count_picks(dve, lk):
            for rank, (sc, top) in enumerate(((score, top1), (rest, top2))):
                lk.link(nc.vector.tensor_tensor(pick[:, :, :], sc[:, :, :], over_experts(top[:, :]), ALU.is_equal))
                lk.link(nc.vector.tensor_tensor(pick[:, :, :], pick[:, :, :], over_pixels(order[:, :]), ALU.mult))
                lk.link(nc.vector.tensor_reduce(pick_max[:, :], pick[:, :, :], AX.X, ALU.max))
                lk.link(nc.vector.tensor_tensor(onehot[:, rank], pick[:, :, :], over_experts(pick_max[:, :]),
                                                ALU.is_equal))
                if rank == 0:
                    lk.link(nc.vector.scalar_tensor_tensor(
                        rest[:, :, :], onehot[:, 0], -2.0, score[:, :, :], ALU.mult, ALU.add))
            for rank in range(2):
                ins = nc.vector.tensor_tensor(onehot[:, rank], onehot[:, rank], over_experts(valid[:, :]), ALU.mult)
                lk.inc(ins)
            lk.wait()
            lk.link(nc.vector.tensor_reduce(cnt_img[:, :, :], onehot[:, :, :, :].rearrange("p r c e -> p r e c"),
                                            AX.X, ALU.add))

        def sum_counts(pe, s):
            pe.wait_ge(s.cnt_ready, 1)
            nc.tensor.matmul(g_ps[:, 0:2 * E], ones[:, :], cnt[:, :, :].rearrange("p r e -> p (r e)"),
                             start=True, stop=True).then_inc(s.cnt_summed, 1)

        def find_present(dve, s, lk):
            dve.wait_ge(s.cnt_summed, 1)
            lk.link(nc.vector.tensor_scalar(present[:, :], g_ps[:, 0:2 * E], 0.5, None, ALU.is_gt))


        def mm1(pe, b, par, u, first=False, chunks=range(NK)):
            h, e = divmod(u, E)
            if first:
                pe.wait_ge(wlo_ready, 1)
                pe.wait_ge(main.xlo_ready, 1)
            elif isinstance(b, int) and b == 0 and h == 0:
                pe.wait_ge(wlo_ready, 1 + e)
            elif e == 0:
                pe.wait_ge(main.xlo_ready, HALVES * b + h + 1)
            for k in chunks:
                if not first:
                    pe.wait_ge(relu_done, CHUNKS * b + NK * u + k - (ZB - 1))
                z = z_ps[:, (NK * u + k) % ZB, 0:T]
                ks = slice(k * P, (k + 1) * P)
                for j in range(NJ):
                    hi, lo = x_hi[:, par, h, j], x_lo[:, par, h, j]
                    nc.tensor.matmul(z, w1_hi[:, e, j, ks], lo, start=(j == 0), stop=False)
                    nc.tensor.matmul(z, w1_lo[:, e, j, ks], hi, start=False, stop=False)
                    ins = nc.tensor.matmul(z, w1_hi[:, e, j, ks], hi, start=False, stop=(j == NJ - 1))
                ins.then_inc(z_ready, 1)

        def mm2(pe, b, u, tail=False):
            h, e = divmod(u, E)
            if isinstance(b, int) and b == 0 and h == 0:
                pe.wait_ge(wlo_ready, 1 + E + e)
            if e == 0:
                pe.wait_ge(out_ready, HALVES * b + h)
            for k in range(NK):
                slot = (NK * u + k) % RING
                pe.wait_ge(hlo_ready, CHUNKS * b + NK * u + k + 1)
                for m in range(NJ):
                    y = y_ps[:, m, 0:T]
                    ms = slice(m * P, (m + 1) * P)
                    first, last = e == 0 and k == 0, e == E - 1 and k == NK - 1
                    nc.tensor.matmul(y, w2_hi[:, e, k, ms], h_lo[:, slot], start=first, stop=False)
                    nc.tensor.matmul(y, w2_lo[:, e, k, ms], h_hi[:, slot], start=False, stop=False)
                    ins = nc.tensor.matmul(y, w2_hi[:, e, k, ms], h_hi[:, slot], start=False, stop=last)
                    if tail and k == NK - 1:
                        ins.then_inc(tail_product, 1)
            if tail:
                return
            ins.then_inc(unit_done, 1)

        def relu(act, b, q):
            e = (q // NK) % E
            act.wait_ge(z_ready, CHUNKS * b + q + 1)
            nc.scalar.activation(hid[:, q % RING], z_ps[:, q % ZB, 0:T], ACT.Relu,
                                 bias=b1_sb[:, e, q % NK:q % NK + 1]).then_inc(relu_done, 1)

        def split_h_hi(act, b, q):
            act.wait_ge(scaled, CHUNKS * b + q + 1)
            nc.scalar.copy(h_hi[:, q % RING], hid[:, q % RING]).then_inc(hhi_ready, 1)

        def scale(dve, b, q):
            img = q // CHUNKS
            u = (q % CHUNKS) // NK
            h, e = divmod(u, E)
            if isinstance(b, int) and b == 0 and q in (0, NK):
                dve.wait_ge((first_row_loaded, rows_loaded[0])[u], 16)
            elif e == 0 and q % NK == 0:
                dve.wait_ge(rows_loaded[h], 16 * (b + img + 1))
            dve.wait_ge(relu_done, CHUNKS * b + q + 1)
            nc.vector.tensor_tensor(hid[:, q % RING], hid[:, q % RING], rows[:, h, e],
                                    ALU.mult).then_inc(scaled, 1)

        def split_h_lo(dve, b, q):
            dve.wait_ge(hhi_ready, CHUNKS * b + q + 1)
            nc.vector.tensor_tensor(h_lo[:, q % RING], hid[:, q % RING], h_hi[:, q % RING].bitcast(f32),
                                    ALU.subtract).then_inc(hlo_ready, 1)

        def add_bias(dve, par, h, rank, lk):
            for m in range(NJ):
                xs = x_raw[:, par, m, half(h)]
                lk.inc(nc.vector.scalar_tensor_tensor(xs, rows[:, h, E + rank], bias01[:, rank, m:m + 1], xs,
                                                      ALU.mult, ALU.add))

        def add_product(dve, b, par, h):
            dve.wait_ge(unit_done, UNITS * b + E * (h + 1))
            xs = x_raw[:, par, :, half(h)]
            nc.vector.tensor_tensor(xs, xs, y_ps[:, :, 0:T], ALU.add).then_inc(out_ready, 1)

        def store(sp, b, par, h):
            sp.wait_ge(out_ready, HALVES * b + h + 1)
            sp.dma_start(out_v[b][:, :, half(h)], x_raw[:, par, :, half(h)]).then_inc(stored, 16)

        def rows_out(sp, n, lk_value):
            sp.wait_ge(dve_step, lk_value)
            sp.dma_start(rows_dram.rearrange("r (g i) -> g r i", g=4), wrow[:, 0:QUART]).then_inc(rows_written, 16)

        def rows_in(sp, n, h):
            sp.wait_ge(rows_written, 16 * n + 16)
            sp.dma_start(rows[:, h], rows_dram[0:ROWS, half(h)].unsqueeze(0).to_broadcast([P, ROWS, T])
                         ).then_inc(rows_loaded[h], 16)

        def each_image(eng, image):
            image(0, 0, True, False)
            with eng.Fori(0, (B - 2) // 2) as i:
                image(i * 2 + 1, 1, False, False)
                image(i * 2 + 2, 0, False, False)
            image(B - 1, (B - 1) % 2, False, True)

        START, FIRST_ROWS, IMAGE_ROWS = [], [], []

        block = ctx.enter_context(nc.Block())

        @block.vector
        def _(dve):
            lk = Links(dve, dve_step, 0)
            nc.vector.memset(st[:, :, :], 1.0)
            nc.vector.memset(minus_half[:, :], -0.5)
            nc.vector.memset(ones[:, :], 1.0)
            nc.vector.memset(gw_part[:, :, :], 0.0)
            nc.vector.memset(lg_rows[:, :], 0.0)
            nc.vector.memset(wpix[:, :, :], 0.0)
            nc.vector.memset(valid[:, 0:GJ - 1], 1.0)
            nc.vector.memset(valid[:, GJ - 1:GJ], 0.0).then_inc(const_ready, 1)
            dve.wait_ge(const_ready, 1)
            for g in range(4):
                nc.vector.memset(valid[32 * g:32 * g + QUART % 32, GJ - 1:GJ], 1.0)
            for e in range(E):
                ins = nc.vector.memset(order[:, e:e + 1], float(E - e))
            ins.then_inc(const_ready, 1)
            dve.wait_ge(const_ready, 2)

            for i in range(NJ * HALVES):
                dve.wait_ge(first_loaded[i // HALVES], 16)
                ins = nc.vector.bn_stats(st6[:, i], x_raw[:, 0, i // HALVES, half(i % HALVES)])
            lk.inc(ins)
            group_stats(dve, main, 0, lk)
            dve.wait_ge(small_loaded, 64)
            lk.link(nc.vector.tensor_copy(gw_part[:, :, 0:E], gw_in[:, :, :]))
            lk.link(nc.vector.tensor_tensor(gw_rest[:, 0], gw_in[:, :, :], gw_part[:, :, 0:E], ALU.subtract))
            lk.link(nc.vector.tensor_copy(gw_part[:, :, E:2 * E], gw_rest[:, 0]))
            nc.vector.tensor_tensor(gw_part[:, :, 2 * E:3 * E], gw_rest[:, 0], gw_part[:, :, E:2 * E],
                                    ALU.subtract).then_inc(gw_ready, 1)
            norm_columns(dve, main, 0, lk)
            for h in range(HALVES):
                normalise(dve, main, 0, 0, h, True)
            for h in range(HALVES):
                less_part1(dve, main, 0, h, True)
            for h in range(HALVES):
                part3(dve, main, 0, h, True)
            for h in range(HALVES):
                split_x_lo(dve, main, 0, 0, h, True)
            gate_logits(dve, main, 0, lk)
            gate_top2(dve, main, 0, lk)
            gate_gap(dve)
            count_picks(dve, lk)
            nc.vector.tensor_copy(cnt[:, :, :], cnt_img[:, :, :]).then_inc(main.cnt_ready, 1)
            gate_weights(dve, 0, lk)
            find_present(dve, main, lk)
            lk.link(nc.vector.tensor_reduce(fewest[:, :], present[:, :], AX.X, ALU.min))
            nc.vector.tensor_scalar(missing[:, :], fewest[:, :], -1.0, 1.0, ALU.mult, ALU.add).then_inc(flag_ready, 1)
            dve.wait_ge(flag_ready, 1)
            flag = dve.value_load(missing[0:1, 0:1], min_val=0, max_val=1)
            with dve.If(flag > 0):
                nc.vector.memset(pad[:, :], 0.0).then_inc(scan_free, 1)
                with dve.Fori(1, B) as b:
                    n = b - 1
                    sk = Links(dve, scan_step, n * SCAN_LINKS)
                    for h in range(HALVES):
                        stats(dve, scan, b, 1, h, sk)
                    group_stats(dve, scan, n, sk)
                    norm_columns(dve, scan, n, sk)
                    for h in range(HALVES):
                        normalise(dve, scan, n, 1, h)
                        less_part1(dve, scan, n, h)
                        part3(dve, scan, n, h)
                    gate_logits(dve, scan, n, sk)
                    gate_top2(dve, scan, n, sk)
                    count_picks(dve, sk)
                    nc.vector.tensor_tensor(cnt[:, :, :], cnt[:, :, :], cnt_img[:, :, :],
                                            ALU.add).then_inc(scan_free, 1)
                    assert sk.n == SCAN_LINKS, sk.n
                dve.wait_ge(scan_free, B)
                nc.vector.tensor_copy(cnt_img[:, :, :], cnt[:, :, :]).then_inc(scan.cnt_ready, 1)
                sk = Links(dve, scan_step, (B - 1) * SCAN_LINKS)
                find_present(dve, scan, sk)

            gate_coefs(lk)
            FIRST_ROWS.append(lk.n)
            for rank in range(2):
                lk.inc(nc.vector.tensor_scalar(bias01[:, rank], b2_sb[:, 0], present[:, E * rank:E * rank + 1],
                                               None, ALU.mult))
            for e in range(1, E):
                lk.wait()
                for rank in range(2):
                    lk.inc(nc.vector.scalar_tensor_tensor(
                        bias01[:, rank], b2_sb[:, e], present[:, E * rank + e:E * rank + e + 1],
                        bias01[:, rank], ALU.mult, ALU.add))
            lk.wait()
            START.append(lk.n)
            scale(dve, 0, 0)

            def image(b, par, first, last):
                nxt = 1 - par
                n = b + 1
                lk = Links(dve, dve_step, DVE_LINKS * b + START[0])
                for q in range(CHUNKS):
                    if q == NK - 1 and not first:
                        add_product(dve, b - 1, nxt, 1)
                    if q == E * NK + NK - 1:
                        add_product(dve, b, par, 0)
                    if not (last and q == CHUNKS - 1):
                        scale(dve, b, q + 1)
                    split_h_lo(dve, b, q)
                    if q in (4, 22):
                        for rank in range(2):
                            add_bias(dve, par, q // (E * NK), rank, lk)
                            lk.wait()
                    if last:
                        continue
                    if q == 5:
                        stats(dve, main, n, nxt, 0, lk)
                    if q == 7:
                        stats(dve, main, n, nxt, 1, lk)
                        group_stats(dve, main, n, lk)
                    if q == 10:
                        norm_columns(dve, main, n, lk)
                        normalise(dve, main, n, nxt, 0)
                        less_part1(dve, main, n, 0)
                    if q == 13:
                        split_x_lo(dve, main, n, nxt, 0)
                        dve.wait_ge(main.xlo_ready, HALVES * n + 1)
                        normalise(dve, main, n, nxt, 1)
                        part3(dve, main, n, 0)
                    if q == 14:
                        dve.wait_ge(main.part3_ready, HALVES * n + 1)
                        less_part1(dve, main, n, 1)
                    if q == 16:
                        part3(dve, main, n, 1)
                        split_x_lo(dve, main, n, nxt, 1)
                        gate_logits(dve, main, n, lk)
                    if q == 17:
                        gate_top2(dve, main, n, lk)
                        gate_gap(dve)
                    if q == 19:
                        gate_weights(dve, n, lk)
                        gate_coefs(lk)
                        IMAGE_ROWS.append(lk.n)
                if not last:
                    assert lk.n == DVE_LINKS, lk.n
                else:
                    for m in range(NJ):
                        dve.wait_ge(tail_product, m + 1)
                        xs = x_raw[:, par, m, half(1)]
                        nc.vector.tensor_tensor(xs, xs, y_ps[:, m, 0:T], ALU.add).then_inc(tail_ready, 1)

            each_image(dve, image)

        @block.scalar
        def _(act):
            def weight_hi(which, e):
                src, hi, loaded = ((w1_in, w1_hi, w1_loaded), (w2_in, w2_hi, w2_loaded))[which]
                act.wait_ge(loaded[e], 16)
                nc.scalar.copy(hi[:, e].rearrange("p j d -> p (j d)"), src[e]).then_inc(whi_ready, 1)

            for e in range(3):
                weight_hi(0, e)
            for h in range(HALVES):
                part1(act, main, 0, h, True)
            for h in range(HALVES):
                part2(act, main, 0, h, True)
            for h in range(HALVES):
                split_x_hi(act, main, 0, 0, h, True)
            weight_hi(0, 3)
            gate_copy(act, main, 0)
            gate_exp(act, main, 0)
            weight_hi(1, 0)
            act.wait_ge(main.xlo_ready, HALVES)
            relu(act, 0, 0)
            gate_gap_exp(act, 0)
            relu(act, 0, 1)
            weight_hi(1, 1)
            for q in range(2, AHEAD * NK):
                relu(act, 0, q)
            for e in range(2, E):
                weight_hi(1, e)
            act.wait_ge(flag_ready, 1)
            flag = act.value_load(missing[0:1, 0:1], min_val=0, max_val=1)
            with act.If(flag > 0):
                with act.Fori(1, B) as b:
                    n = b - 1
                    for h in range(HALVES):
                        part1(act, scan, n, h)
                        part2(act, scan, n, h)
                    gate_copy(act, scan, n)
                    gate_exp(act, scan, n)

            def image(b, par, first, last):
                nxt = 1 - par
                n = b + 1
                for q in range(CHUNKS):
                    if first and q + 1 == RING:
                        act.wait_ge(unit_done, 1)
                    if not (last and q == CHUNKS - 1) and not (first and q + 1 < AHEAD * NK):
                        relu(act, b, q + 1)
                    split_h_hi(act, b, q)
                    if last:
                        continue
                    if q == 10:
                        part1(act, main, n, 0)
                        split_x_hi(act, main, n, nxt, 0)
                    if q == 11:
                        part2(act, main, n, 0)
                    if q == 13:
                        part1(act, main, n, 1)
                    if q == 14:
                        split_x_hi(act, main, n, nxt, 1)
                    if q == 16:
                        part2(act, main, n, 1)
                        gate_copy(act, main, n)
                        gate_exp(act, main, n)
                    if q == 18:
                        gate_gap_exp(act, n)

            each_image(act, image)

        @block.gpsimd
        def _(pool):
            pool.wait_ge(const_ready, 1)
            inverse_std(pool, main, 0)
            def weight_lo(which, e):
                src, hi, lo = ((w1_in, w1_hi, w1_lo), (w2_in, w2_hi, w2_lo))[which]
                pool.wait_ge(whi_ready, 1 + E * which + e)
                nc.gpsimd.tensor_tensor(lo[:, e].rearrange("p j d -> p (j d)"), src[e],
                                        hi[:, e].rearrange("p j d -> p (j d)").bitcast(f32),
                                        ALU.subtract).then_inc(wlo_ready, 1)

            for e in range(E):
                weight_lo(0, e)
            for e in range(E):
                weight_lo(1, e)
            pool.wait_ge(flag_ready, 1)
            flag = pool.value_load(missing[0:1, 0:1], min_val=0, max_val=1)
            with pool.If(flag > 0):
                with pool.Fori(1, B) as b:
                    inverse_std(pool, scan, b - 1)
            with pool.Fori(1, B) as b:
                inverse_std(pool, main, b)

        @block.sync
        def _(sp):
            for j in range(NJ):
                sp.dma_start(x_raw[:, 0, j], x_v[0][:, j]).then_inc(first_loaded[j], 16)
            sp.dma_start(w1_in[0], w1[:, 0]).then_inc(w1_loaded[0], 16)
            sp.dma_start(gw_in[:, :, :], gate_w.rearrange("(p j) e -> p j e", j=NJ)).then_inc(small_loaded, 16)
            sp.dma_start(gb[:, :], gate_b.unsqueeze(0).to_broadcast([P, E])).then_inc(small_loaded, 16)
            sp.dma_start(b1_sb[:, :, :], b1).then_inc(small_loaded, 16)
            sp.dma_start(b2_sb[:, :, :], b2).then_inc(small_loaded, 16)
            for e in range(1, E):
                sp.dma_start(w1_in[e], w1[:, e]).then_inc(w1_loaded[e], 16)
            for e in range(E):
                if e >= 2:
                    sp.wait_ge(wlo_ready, 1 + E + e - 2)
                sp.dma_start(w2_in[e], w2[:, e]).then_inc(w2_loaded[e], 16)
            sp.wait_ge(flag_ready, 1)
            flag = sp.value_load(missing[0:1, 0:1], min_val=0, max_val=1)
            with sp.If(flag > 0):
                sp.wait_ge(wlo_ready, 2 * E)
                with sp.Fori(1, B) as b:
                    sp.wait_ge(scan_free, b)
                    for h in range(HALVES):
                        load_x(sp, scan, b, 1, h)
            rows_out(sp, 0, FIRST_ROWS[0])
            sp.wait_ge(wlo_ready, E)
            sp.wait_ge(rows_written, 16)
            for lo, hi, loaded in ((0, 1, first_row_loaded), (1, ROWS, rows_loaded[0])):
                sp.dma_start(rows[:, 0, lo:hi], rows_dram[lo:hi, half(0)].unsqueeze(0).to_broadcast([P, hi - lo, T])
                             ).then_inc(loaded, 16)
            rows_in(sp, 0, 1)

            def image(b, par, first, last):
                nxt = 1 - par
                n = b + 1
                if not last:
                    if first:
                        sp.wait_ge(wlo_ready, 2 * E)
                    else:
                        sp.wait_ge(stored, 16 * (HALVES * b - 1))
                    load_x(sp, main, n, nxt, 0)
                if not first:
                    store(sp, b - 1, nxt, 1)
                    if not last:
                        sp.wait_ge(stored, 16 * HALVES * b)
                    sp.wait_ge(scaled, CHUNKS * b + 1)
                    rows_in(sp, b, 1)
                if not last:
                    load_x(sp, main, n, nxt, 1)
                store(sp, b, par, 0)
                if not last:
                    rows_out(sp, n, DVE_LINKS * b + START[0] + IMAGE_ROWS[0])
                    sp.wait_ge(scaled, CHUNKS * b + E * NK)
                    rows_in(sp, n, 0)

            each_image(sp, image)
            for m in range(NJ):
                sp.wait_ge(tail_ready, m + 1)
                sp.dma_start(out_v[B - 1][:, m, half(1)], x_raw[:, (B - 1) % 2, m, half(1)]).then_inc(stored, 16)
            sp.wait_ge(stored, 16 * (HALVES * B - 1 + NJ))

        @block.tensor
        def _(pe):
            pe.wait_ge(gw_ready, 1)
            pe.wait_ge(main.part1_ready, 1)
            for _ in range(WARM):
                nc.tensor.matmul(g_ps[:, 0:P], ones[:, :], ones[:, :], start=True, stop=True)
            gate_product(pe, main, 0)
            mm1(pe, 0, 0, 0, first=True)
            sum_counts(pe, main)
            for u in range(1, AHEAD + 1):
                mm1(pe, 0, 0, u)
            mm1(pe, 0, 0, AHEAD + 1, chunks=range(1))
            pe.wait_ge(flag_ready, 1)
            flag = pe.value_load(missing[0:1, 0:1], min_val=0, max_val=1)
            with pe.If(flag > 0):
                with pe.Fori(1, B) as b:
                    gate_product(pe, scan, b - 1)
                sum_counts(pe, scan)

            def image(b, par, first, last):
                nxt = 1 - par
                n = b + 1
                for u in range(UNITS):
                    if u == 5 and not last:
                        mm1(pe, b, par, u + 1, chunks=range(1))
                        gate_product(pe, main, n)
                        mm1(pe, b, par, u + 1, chunks=range(1, NK))
                    elif u < UNITS - 1:
                        if not (first and u < AHEAD):
                            mm1(pe, b, par, u + 1, chunks=range(1 if first and u == AHEAD else 0, NK))
                    elif not last:
                        mm1(pe, b + 1, nxt, 0)
                    mm2(pe, b, u, tail=last and u == UNITS - 1)

            each_image(pe, image)




def kernel(x, L0_conv_gate_w, L0_conv_gate_b, L0_conv_w1, L0_conv_b1, L0_conv_w2, L0_conv_b2):
    import numpy as np
    import concourse.bacc as bacc
    from concourse.bass_utils import run_bass_kernel_spmd

    w1 = np.asarray(L0_conv_w1).reshape(E, HID, P, NJ).transpose(2, 0, 3, 1)
    w2 = np.asarray(L0_conv_w2).reshape(E, P, NJ, NK, P).transpose(4, 0, 3, 2, 1).reshape(P, E, NK, C)
    b1 = np.asarray(L0_conv_b1).reshape(E, NK, P).transpose(2, 0, 1)
    b2 = np.asarray(L0_conv_b2).reshape(E, P, NJ).transpose(1, 0, 2)
    arrays = {"x": x, "gate_w": L0_conv_gate_w, "gate_b": L0_conv_gate_b, "w1": w1, "b1": b1, "w2": w2, "b2": b2}
    arrays = {f"in_{k}": np.ascontiguousarray(v) for k, v in arrays.items()}

    nc = bacc.Bacc("TRN2", target_bir_lowering=False, num_devices=1)
    args = [nc.dram_tensor(k, v.shape, mybir.dt.from_np(v.dtype), kind="ExternalInput").ap()
            for k, v in arrays.items()]
    out = nc.dram_tensor("out", arrays["in_x"].shape, mybir.dt.float32, kind="ExternalOutput").ap()
    conv_moe(nc, *args, out)
    r = run_bass_kernel_spmd(nc, [arrays], core_ids=[0])
    return r.results[0]["out"]
```
